# Optimizing a Trainium2 kernel written in Bass

```python
import numpy as np
import jax
import jax.numpy as jnp

def _softmax(x, axis=-1):
    return jax.nn.softmax(x, axis=axis)

def _gelu(x):
    return jax.nn.gelu(x, approximate=True)

def _silu(x):
    return jax.nn.silu(x)

def _sigmoid(x):
    return jax.nn.sigmoid(x)

def _layernorm(x, axis=-1, eps=1e-05):
    m = jnp.mean(x, axis=axis, keepdims=True)
    v = jnp.var(x, axis=axis, keepdims=True)
    return (x - m) / jnp.sqrt(v + eps)

def _scatter_add(tgt, idx, src, axis=0):
    return tgt.at[idx].add(src)

def _segment_sum(src, seg, n):
    return jax.ops.segment_sum(src, seg, n)
kernel_name = 'mk_xattn_ffn_d2_seqx_r8_d155b2'

def setup_inputs(seed: int=0):
    np.random.seed(seed)
    _w = jnp.asarray

    def _rec_inputs():
        import jax
        import jax.numpy as jnp
        _rk = jax.random.key(seed)
        x = -0.0003929 + 0.9999 * jax.random.normal(jax.random.fold_in(_rk, 1), (4, 512, 128), jnp.float32)
        _lenS = 512 - jax.random.randint(jax.random.fold_in(_rk, 7), (4,), 0, max(1, 512 // 4) + 1, jnp.int32)
        _lenS2 = 154 - jax.random.randint(jax.random.fold_in(_rk, 8), (4,), 0, max(1, 154 // 4) + 1, jnp.int32)
        _ctx_768P = jax.random.normal(jax.random.fold_in(_rk, 11), (4, 16, 96), jnp.float32)
        _ctx_768c = jax.random.dirichlet(jax.random.fold_in(_rk, 511), 0.3 * jnp.ones((16,), jnp.float32), (4, 154))
        _ctx_768t = jnp.einsum('bsk,bkd->bsd', _ctx_768c, _ctx_768P)
        _ctx_768t = _ctx_768t * jax.lax.rsqrt(jnp.mean(jnp.square(_ctx_768t)) + 1e-12) * 0.953939
        ctx_768 = 2.09791e-05 + 1.00001 * (_ctx_768t + 0.3 * jax.random.normal(jax.random.fold_in(_rk, 611), (4, 154, 96), jnp.float32))
        return (x, ctx_768)
    x, ctx_768 = _rec_inputs()

    def _L0_xattn_setup():
        import jax, jax.numpy as jnp
        import numpy as np
        QUERY_DIM = 128
        KEY_DIM = 96
        NUM_HEADS = 16
        HEAD_DIM = QUERY_DIM // NUM_HEADS
        SCALE = HEAD_DIM ** (-0.5)
        key = jax.random.key(seed)
        ks = jax.random.split(key, 11)
        B, Nq, Nk = (4, 512, 128)
        s_q = QUERY_DIM ** (-0.5)
        s_k = KEY_DIM ** (-0.5)
        return {'query': jax.random.normal(ks[0], (B, Nq, QUERY_DIM), jnp.float32), 'key': jax.random.normal(ks[1], (B, Nk, KEY_DIM), jnp.float32), 'value': jax.random.normal(ks[2], (B, Nk, KEY_DIM), jnp.float32), 'Wq': jax.random.normal(ks[3], (QUERY_DIM, QUERY_DIM), jnp.float32) * s_q, 'bq': jnp.zeros((QUERY_DIM,), jnp.float32), 'Wk': jax.random.normal(ks[4], (KEY_DIM, QUERY_DIM), jnp.float32) * s_k, 'bk': jnp.zeros((QUERY_DIM,), jnp.float32), 'Wv': jax.random.normal(ks[5], (KEY_DIM, QUERY_DIM), jnp.float32) * s_k, 'bv': jnp.zeros((QUERY_DIM,), jnp.float32), 'Wo': jax.random.normal(ks[6], (QUERY_DIM, QUERY_DIM), jnp.float32) * s_q, 'bo': jnp.zeros((QUERY_DIM,), jnp.float32)}
    _L0_xattn_all = _L0_xattn_setup()
    _L0_xattn_in = {k: v for k, v in _L0_xattn_all.items() if k in ('Wq', 'bq', 'Wk', 'bk', 'Wv', 'bv', 'Wo', 'bo')}
    del _L0_xattn_all

    def _L0_ffn_setup():
        import jax, jax.numpy as jnp
        import numpy as np
        H = 128
        E = 8
        B, S = (4, 256)
        key = jax.random.key(seed)
        k1, k2, k3, k4 = jax.random.split(key, 4)
        x = jax.random.normal(k1, (B, S, H), dtype=jnp.float32)
        wg = jax.random.normal(k2, (H, E), dtype=jnp.float32) * 0.02
        W = jax.random.normal(k3, (E, H, H), dtype=jnp.float32) * 0.02
        b = jax.random.normal(k4, (E, H), dtype=jnp.float32) * 0.02
        return {'x': x, 'wg': wg, 'W': W, 'b': b}
    _L0_ffn_all = _L0_ffn_setup()
    _L0_ffn_in = {k: v for k, v in _L0_ffn_all.items() if k in ('wg', 'W', 'b')}
    del _L0_ffn_all

    def _L1_xattn_setup():
        import jax, jax.numpy as jnp
        import numpy as np
        HEADS = 8
        DIM_HEAD = 64
        SCALE = DIM_HEAD ** (-0.5)
        key = jax.random.key(seed)
        ks = jax.random.split(key, 7)
        B, Nq, Nc = (4, 256, 256)
        Dq, Dc = (128, 96)
        inner = HEADS * DIM_HEAD
        x = jax.random.normal(ks[0], (B, Nq, Dq), dtype=jnp.float32)
        context = jax.random.normal(ks[1], (B, Nc, Dc), dtype=jnp.float32)
        Wq = jax.random.normal(ks[2], (Dq, inner), dtype=jnp.float32) * Dq ** (-0.5)
        Wk = jax.random.normal(ks[3], (Dc, inner), dtype=jnp.float32) * Dc ** (-0.5)
        Wv = jax.random.normal(ks[4], (Dc, inner), dtype=jnp.float32) * Dc ** (-0.5)
        Wo = jax.random.normal(ks[5], (inner, Dq), dtype=jnp.float32) * inner ** (-0.5)
        bo = jax.random.normal(ks[6], (Dq,), dtype=jnp.float32) * 0.01
        return {'x': x, 'context': context, 'Wq': Wq, 'Wk': Wk, 'Wv': Wv, 'Wo': Wo, 'bo': bo}
    _L1_xattn_all = _L1_xattn_setup()
    _L1_xattn_in = {k: v for k, v in _L1_xattn_all.items() if k in ('Wq', 'Wk', 'Wv', 'Wo', 'bo')}
    del _L1_xattn_all

    def _L1_ffn_setup():
        import jax, jax.numpy as jnp
        import numpy as np
        DIM = 128
        N_EXPERTS = 16
        TOP_K = 4
        N_GROUP = 4
        TOPK_GROUP = 2
        MOE_INTER = 64
        SHARED_INTER = 256
        ROUTED_SCALE = 2.5

        def relu2(x):
            return jnp.square(jax.nn.relu(x))

        def _router(x2, gate_w, bias_e):
            T = x2.shape[0]
            logits = x2 @ gate_w.T
            scores = jax.nn.sigmoid(logits)
            sc = jax.lax.stop_gradient(scores + bias_e[None, :])
            grp = sc.reshape(T, N_GROUP, N_EXPERTS // N_GROUP)
            top2, _ = jax.lax.top_k(grp, 2)
            group_scores = top2.sum(-1)
            _, gidx = jax.lax.top_k(group_scores, TOPK_GROUP)
            rows = jnp.arange(T)[:, None]
            gmask = jnp.zeros((T, N_GROUP), dtype=sc.dtype).at[rows, gidx].set(1.0)
            smask = jnp.repeat(gmask, N_EXPERTS // N_GROUP, axis=1)
            masked = jnp.where(smask > 0, sc, 0.0)
            _, topk_idx = jax.lax.top_k(masked, TOP_K)
            topk_w = jnp.take_along_axis(scores, topk_idx, axis=1)
            topk_w = topk_w / (topk_w.sum(-1, keepdims=True) + 1e-20)
            topk_w = topk_w * ROUTED_SCALE
            return (topk_idx, topk_w)
        key = jax.random.key(seed)
        ks = jax.random.split(key, 6)
        hidden_states = jax.random.normal(ks[0], (2, 256, DIM), dtype=jnp.float32)
        gate_w = jax.random.normal(ks[1], (N_EXPERTS, DIM), dtype=jnp.float32) * 0.02
        bias_e = jnp.zeros((N_EXPERTS,), dtype=jnp.float32)
        up_w = jax.random.normal(ks[2], (N_EXPERTS, MOE_INTER, DIM), dtype=jnp.float32) * 0.02
        down_w = jax.random.normal(ks[3], (N_EXPERTS, DIM, MOE_INTER), dtype=jnp.float32) * 0.02
        shared_up = jax.random.normal(ks[4], (SHARED_INTER, DIM), dtype=jnp.float32) * 0.02
        shared_down = jax.random.normal(ks[5], (DIM, SHARED_INTER), dtype=jnp.float32) * 0.02
        return {'hidden_states': hidden_states, 'gate_w': gate_w, 'bias_e': bias_e, 'up_w': up_w, 'down_w': down_w, 'shared_up': shared_up, 'shared_down': shared_down}
    _L1_ffn_all = _L1_ffn_setup()
    _L1_ffn_in = {k: v for k, v in _L1_ffn_all.items() if k in ('gate_w', 'bias_e', 'up_w', 'down_w', 'shared_up', 'shared_down')}
    del _L1_ffn_all
    return {'x': x, 'ctx_768': ctx_768, 'L0_xattn_Wq': _L0_xattn_in['Wq'], 'L0_xattn_bq': _L0_xattn_in['bq'], 'L0_xattn_Wk': _L0_xattn_in['Wk'], 'L0_xattn_bk': _L0_xattn_in['bk'], 'L0_xattn_Wv': _L0_xattn_in['Wv'], 'L0_xattn_bv': _L0_xattn_in['bv'], 'L0_xattn_Wo': _L0_xattn_in['Wo'], 'L0_xattn_bo': _L0_xattn_in['bo'], 'L0_ffn_wg': _L0_ffn_in['wg'], 'L0_ffn_W': _L0_ffn_in['W'], 'L0_ffn_b': _L0_ffn_in['b'], 'L1_xattn_Wq': _L1_xattn_in['Wq'], 'L1_xattn_Wk': _L1_xattn_in['Wk'], 'L1_xattn_Wv': _L1_xattn_in['Wv'], 'L1_xattn_Wo': _L1_xattn_in['Wo'], 'L1_xattn_bo': _L1_xattn_in['bo'], 'L1_ffn_gate_w': _L1_ffn_in['gate_w'], 'L1_ffn_bias_e': _L1_ffn_in['bias_e'], 'L1_ffn_up_w': _L1_ffn_in['up_w'], 'L1_ffn_down_w': _L1_ffn_in['down_w'], 'L1_ffn_shared_up': _L1_ffn_in['shared_up'], 'L1_ffn_shared_down': _L1_ffn_in['shared_down']}

def reference(x, ctx_768, L0_xattn_Wq, L0_xattn_bq, L0_xattn_Wk, L0_xattn_bk, L0_xattn_Wv, L0_xattn_bv, L0_xattn_Wo, L0_xattn_bo, L0_ffn_wg, L0_ffn_W, L0_ffn_b, L1_xattn_Wq, L1_xattn_Wk, L1_xattn_Wv, L1_xattn_Wo, L1_xattn_bo, L1_ffn_gate_w, L1_ffn_bias_e, L1_ffn_up_w, L1_ffn_down_w, L1_ffn_shared_up, L1_ffn_shared_down):
    import jax
    import jax.numpy as jnp

    def _L0_xattn_ref(query, key, value, Wq, bq, Wk, bk, Wv, bv, Wo, bo):
        import jax, jax.numpy as jnp
        import numpy as np
        QUERY_DIM = 128
        KEY_DIM = 96
        NUM_HEADS = 16
        HEAD_DIM = QUERY_DIM // NUM_HEADS
        SCALE = HEAD_DIM ** (-0.5)
        B, Nq, _ = query.shape
        Nk = key.shape[1]
        q = (query @ Wq + bq).reshape(B, Nq, NUM_HEADS, HEAD_DIM).transpose(0, 2, 1, 3)
        k = (key @ Wk + bk).reshape(B, Nk, NUM_HEADS, HEAD_DIM).transpose(0, 2, 1, 3)
        v = (value @ Wv + bv).reshape(B, Nk, NUM_HEADS, HEAD_DIM).transpose(0, 2, 1, 3)
        attn = jnp.einsum('bhqd,bhkd->bhqk', q, k) * SCALE
        attn = jax.nn.softmax(attn, axis=-1)
        out = jnp.einsum('bhqk,bhkd->bhqd', attn, v)
        out = out.transpose(0, 2, 1, 3).reshape(B, Nq, QUERY_DIM)
        return out @ Wo + bo

    def _L0_ffn_ref(x, wg, W, b):
        import jax, jax.numpy as jnp
        import numpy as np
        H = 128
        E = 8
        B, S = (4, 256)
        Bb, Ss, Hh = x.shape
        Ee = wg.shape[1]
        T = Bb * Ss
        C = T // Ee
        xt = x.reshape(T, Hh)
        logits = xt @ wg
        probs = jax.nn.softmax(logits, axis=-1)
        idx = jnp.argmax(probs, axis=-1)
        mask = jax.nn.one_hot(idx, Ee, dtype=xt.dtype)
        locations = jnp.cumsum(mask, axis=0) - mask
        mask = mask * (locations < C).astype(xt.dtype)
        gate = jnp.sum(probs * mask, axis=-1)
        loc_s = jnp.sum(locations * mask, axis=-1).astype(jnp.int32)
        loc_oh = jax.nn.one_hot(loc_s, C, dtype=xt.dtype)
        dispatch = mask[:, :, None] * loc_oh[:, None, :]
        combine = gate[:, None, None] * dispatch
        exp_in = jnp.einsum('tec,th->ech', dispatch, xt)
        exp_out = jnp.einsum('ech,efh->ecf', exp_in, W) + b[:, None, :]
        out = jnp.einsum('tec,ecf->tf', combine, exp_out)
        return out.reshape(Bb, Ss, Hh)

    def _L1_xattn_ref(x, context, Wq, Wk, Wv, Wo, bo):
        import jax, jax.numpy as jnp
        import numpy as np
        HEADS = 8
        DIM_HEAD = 64
        SCALE = DIM_HEAD ** (-0.5)
        B, Nq, _ = x.shape
        q = (x @ Wq).reshape(B, Nq, HEADS, DIM_HEAD)
        k = (context @ Wk).reshape(B, context.shape[1], HEADS, DIM_HEAD)
        v = (context @ Wv).reshape(B, context.shape[1], HEADS, DIM_HEAD)
        sim = jnp.einsum('bihd,bjhd->bhij', q, k) * SCALE
        attn = jax.nn.softmax(sim, axis=-1)
        out = jnp.einsum('bhij,bjhd->bihd', attn, v)
        out = out.reshape(B, Nq, HEADS * DIM_HEAD)
        return out @ Wo + bo

    def _L1_ffn_ref(hidden_states, gate_w, bias_e, up_w, down_w, shared_up, shared_down):
        import jax, jax.numpy as jnp
        import numpy as np
        DIM = 128
        N_EXPERTS = 16
        TOP_K = 4
        N_GROUP = 4
        TOPK_GROUP = 2
        MOE_INTER = 64
        SHARED_INTER = 256
        ROUTED_SCALE = 2.5

        def relu2(x):
            return jnp.square(jax.nn.relu(x))

        def _router(x2, gate_w, bias_e):
            T = x2.shape[0]
            logits = x2 @ gate_w.T
            scores = jax.nn.sigmoid(logits)
            sc = jax.lax.stop_gradient(scores + bias_e[None, :])
            grp = sc.reshape(T, N_GROUP, N_EXPERTS // N_GROUP)
            top2, _ = jax.lax.top_k(grp, 2)
            group_scores = top2.sum(-1)
            _, gidx = jax.lax.top_k(group_scores, TOPK_GROUP)
            rows = jnp.arange(T)[:, None]
            gmask = jnp.zeros((T, N_GROUP), dtype=sc.dtype).at[rows, gidx].set(1.0)
            smask = jnp.repeat(gmask, N_EXPERTS // N_GROUP, axis=1)
            masked = jnp.where(smask > 0, sc, 0.0)
            _, topk_idx = jax.lax.top_k(masked, TOP_K)
            topk_w = jnp.take_along_axis(scores, topk_idx, axis=1)
            topk_w = topk_w / (topk_w.sum(-1, keepdims=True) + 1e-20)
            topk_w = topk_w * ROUTED_SCALE
            return (topk_idx, topk_w)
        B, S, D = hidden_states.shape
        x2 = hidden_states.reshape(-1, D)
        T = x2.shape[0]
        topk_idx, topk_w = _router(x2, gate_w, bias_e)
        rows = jnp.arange(T)[:, None]
        combine = jnp.zeros((T, N_EXPERTS), dtype=topk_w.dtype).at[rows, topk_idx].add(topk_w)

        def body(acc, inp):
            wu, wd, cw = inp
            y = relu2(x2 @ wu.T) @ wd.T
            return (acc + cw[:, None] * y, None)
        routed, _ = jax.lax.scan(body, jnp.zeros_like(x2), (up_w, down_w, combine.T))
        shared = relu2(x2 @ shared_up.T) @ shared_down.T
        out = routed + shared
        return out.reshape(B, S, D)
    x = x + _L0_xattn_ref(_layernorm(x, axis=-1), ctx_768, ctx_768, L0_xattn_Wq, L0_xattn_bq, L0_xattn_Wk, L0_xattn_bk, L0_xattn_Wv, L0_xattn_bv, L0_xattn_Wo, L0_xattn_bo)
    x = x + _L0_ffn_ref(_layernorm(x, axis=-1), L0_ffn_wg, L0_ffn_W, L0_ffn_b)
    x = x + _L1_xattn_ref(_layernorm(x, axis=-1), ctx_768, L1_xattn_Wq, L1_xattn_Wk, L1_xattn_Wv, L1_xattn_Wo, L1_xattn_bo)
    x = x + _L1_ffn_ref(_layernorm(x, axis=-1), L1_ffn_gate_w, L1_ffn_bias_e, L1_ffn_up_w, L1_ffn_down_w, L1_ffn_shared_up, L1_ffn_shared_down)
    return x

_drawn_inputs = setup_inputs


def setup_inputs(seed=0):
    import zlib

    import numpy as np

    out = dict(_drawn_inputs(seed))
    spreads = {'L0_xattn_bq': (0.0, 0.349),
     'L0_xattn_bk': (0.0, 0.8),
     'L0_xattn_bv': (0.0, 0.1),
     'L0_xattn_bo': (0.0, 0.1),
     'L1_ffn_bias_e': (0.0, 0.8)}
    factors = {'L0_ffn_b': 8.0,
     'L1_xattn_bo': 6.84,
     'L1_ffn_gate_w': 8.0,
     'L1_ffn_up_w': 6.388,
     'L1_ffn_down_w': 5.693,
     'L1_ffn_shared_up': 3.944,
     'L1_ffn_shared_down': 3.501}
    for name, (base, spread) in spreads.items():
        noise = np.random.default_rng([zlib.crc32(name.encode()), seed]).standard_normal(out[name].shape)
        drawn = base * np.exp(spread * noise) if base else spread * noise
        out[name] = jnp.asarray(drawn.astype(out[name].dtype))
    for name, factor in factors.items():
        out[name] = (out[name] * factor).astype(out[name].dtype)
    return out
```

```python
from contextlib import ExitStack

import concourse.bass as bass
from concourse import mybir

ALU = mybir.AluOpType
ACT = mybir.ActivationFunctionType
AX = mybir.AxisListType.X
F32 = mybir.dt.float32
BF16 = mybir.dt.bfloat16
U32 = mybir.dt.uint32

P = 128
B = 4
NQ = 512
QT = NQ // P
NK = 154
DC = 96
D = 128

H0, HD0 = 16, 8
GH = 4
CH = 5
ROWS = GH * NK
PAIRS0 = H0 // 2
SCALE0 = HD0 ** -0.5
TERMS = [(0, 0), (0, 1), (0, 2), (1, 0), (1, 1), (2, 0)]
KR = len(TERMS) * 2 * HD0
KM = KR + 2
ODD = 52
PW = 3 * P

H1, HD1 = 8, 64
PAIRS1 = H1 // 2
G1 = H1 // GH
SCALE1 = HD1 ** -0.5
FIRST = [128 * j // NK for j in range(CH)]
WIDE = [min(128 * j + 127, ROWS - 1) // NK - FIRST[j] + 1 for j in range(CH)]

E0 = 8
CAP = B * NQ // E0
E1 = 16
NG = 4
HT = 10
RT = 8
UPS = [[0, 1, 2], [3, 4, 5], [6, 7], [8, 9]]
PAD = -1.0e30
HIT = 1.0e30
EPS = 1e-5


def build(nc, x, ctx, wk0, bk0, wv0, bv0, wq0, bq0, wo0, bo0, wg, we, be,
          wq1, wk1, wv1, wo1, bo1, gate_w, bias_e, up_w, down_w, sup_w, sdown_w,
          cf, cb, kones, out):
    qd = nc.dram_tensor("q_parts", [3, P, B, NQ], BF16, kind="Internal").ap()
    kd = nc.dram_tensor("k_parts", [3, P, B, NK], BF16, kind="Internal").ap()
    es = ExitStack()
    with es:
        def sb(name, shape, dt=F32):
            return es.enter_context(nc.sbuf_tensor(name, shape, dt))

        cfs = sb("consts_f", [P, cf.shape[1]])
        cbs = sb("consts_b", [P, cb.shape[1]], BF16)
        ident = cfs[:, 0:P]
        headmask = cfs[:, P:P + CH * GH].rearrange("p (j a) -> p j a", a=GH)
        winmask = cfs[:, P + 20:P + 30].rearrange("p (j w) -> p j w", w=2)
        minus_half = cfs[:, P + 30:P + 34]
        identb = cbs[:, 0:P]
        before = cbs[:, P:2 * P]
        onesb = cbs[:, 2 * P:3 * P]
        sel8 = cbs[:, 3 * P:11 * P].rearrange("p (e c) -> p e c", c=P)
        sel48 = cbs[:, 11 * P:19 * P].rearrange("p (e c) -> p e c", c=P)
        pt0 = sb("pt0", [P, 4, NQ])
        ao0 = sb("ao0", [P, QT, D])
        aoT0 = sb("aoT0", [P, NQ])
        wk0s, wv0s = aoT0[0:DC + 1, 0:D], aoT0[0:DC + 1, D:2 * D]
        wk1s, wv1s = pt0[0:DC, 0, :], pt0[0:DC, 1, :]
        ctx4 = pt0[0:DC + 1, 2:4, :].rearrange("p t n -> p (t n)")[:, 0:CH * P]
        ctxb = pt0[0:NK - P, 2:4, :].rearrange("p t n -> p (t n)")[:, CH * P:CH * P + B * DC]\
            .rearrange("p (b c) -> p b c", b=B)
        ctxa = ao0[:].rearrange("p t n -> p (t n)")[:, 0:B * DC].rearrange("p (b c) -> p b c", b=B)
        wq0s, wo0s, bq0s = sb("wq0s", [P, D]), sb("wo0s", [P, D]), sb("bq0s", [P, 1])
        bo0s, bo1s, biases = sb("bo0s", [P, D]), sb("bo1s", [P, D]), sb("biases", [P, E1])
        wgs, bes = sb("wgs", [P, E0]), sb("bes", [E0, D])
        wq1s = sb("wq1s", [P, 512])
        wo1s = sb("wo1s", [P, 4, D])
        weT = sb("weT", [P, E0, D])
        upT = sb("upT", [P, HT, P])
        gateT = sb("gateT", [P, E1])
        dnT = sb("dnT", [P, HT, D])

        xs = sb("xs", [P, B * QT, D])
        lnT = sb("lnT", [P, B, NQ])
        lnTf = sb("lnTf", [P, NQ])
        xn = sb("xn", [P, QT, D])
        st = sb("st", [P, QT, 6])
        mv = sb("mv", [P, QT, 2])
        ve = sb("ve", [P, B, QT])
        rstd = sb("rstd", [P, B, QT])
        ctxT = sb("ctxT", [DC + 1, B * NK])
        early = lnT[:].rearrange("p b n -> p (b n)")
        kf, kr = early[:, 0:B * NK], early[:, B * NK:2 * B * NK]
        kp = sb("kp", [P, 3, B * NK], BF16)
        qf = early[:, 3 * NQ:4 * NQ]
        qp = sb("qp", [P, 3, NQ], BF16)
        big = sb("big", [P, B * PAIRS0 * NQ // 2])
        qst = big[0:KM, :].bitcast(BF16).rearrange("p (b r n) -> p b r n", b=B, r=PAIRS0)
        keys = sb("keys", [P, B * PAIRS0 * PW // 2])
        kst = keys[0:KM, :].bitcast(BF16).rearrange("p (b r c) -> p b r c", b=B, r=PAIRS0)
        v0 = sb("v0", [P, B, CH, 4, GH, HD0 + 1])
        k1 = sb("k1", [P, B, PAIRS1, 2, NK])
        v1 = sb("v1", [P, B, CH, G1, 2, HD1 + 1])
        mx = sb("mx", [P, QT, H0])
        negm = sb("negm", [H0, NQ], BF16)
        rec0 = sb("rec0", [P, QT, GH])
        hh = keys[:, 0:HT * NQ].rearrange("p (t n) -> p t n", n=NQ)
        mxr = big[:, 0:4 * NQ].rearrange("p (t n) -> p t n", n=NQ)
        rr = big[:, 4 * NQ:9 * NQ].rearrange("p (t n) -> p t n", n=NQ)
        gg = big[:, 9 * NQ:13 * NQ].rearrange("p (t n) -> p t n", n=NQ)
        yT = big[:, 13 * NQ:14 * NQ]
        q1T = big[:, 13 * NQ:14 * NQ].rearrange("p (r n) -> p r n", n=P)
        mx1 = sb("mx1", [P, PAIRS1, 2])
        work = sb("work", [P, 4 * G1 * CH * P])
        s1 = work[:, 0:2 * G1 * CH * P].rearrange("p (t c) -> p t c", t=2)
        pt1 = work[:, 2 * G1 * CH * P:].rearrange("p (t c) -> p t c", t=2)
        rec1 = sb("rec1", [P, G1, GH])
        ao1 = big[:, 14 * NQ:15 * NQ]
        aoT1 = big[:, 15 * NQ:16 * NQ].rearrange("p (c n) -> p c n", n=P)
        qr = work[:, 9 * NQ:10 * NQ]
        oT = work[0:36, 0:NQ]
        nat = work[:, 0:8 * NQ].rearrange("p (t n) -> p t n", n=NQ)
        nat_we = nat[:, 0:2, :].rearrange("p t (e h) -> p (t e) h", h=P)
        nat_up = nat[:, 2:4, :].rearrange("p t (e h) -> p (t e) h", h=P)
        nat_dn = nat[:, 4:6, :].rearrange("p t (e h) -> p (t e) h", h=P)
        nat_sup = nat[:, 6, 0:256].rearrange("p (t h) -> p t h", h=P)
        nat_sdn = nat[:, 6, 256:512].rearrange("p (t h) -> p t h", h=P)
        nat_gw = nat[0:E1, 7, 0:P]
        lsh = sb("lsh", [P, QT, E1])
        lex = sb("lex", [P, QT, E1])
        tick = sb("tick", [P, 2])
        col = sb("col", [P, QT])
        col2 = sb("col2", [P, QT])
        gate = sb("gate", [P, B, QT])
        top = sb("top", [P, QT, 8])
        pin = sb("pin", [P, QT, 16])
        eout = sb("eout", [P, QT, 20])
        pout, gout = eout[:, :, 0:16], eout[:, :, 0:12]
        mk = sb("mk", [P, QT, E0], BF16)
        loc = sb("loc", [P, QT, E0])
        carry = sb("carry", [P, B + 1, E0])
        part = sb("part", [P, QT, P], BF16)
        km = part[:, :, 0:E0]
        c3 = part[:, :, 0:3 * E1].rearrange("p t (s e) -> p t s e", s=3)
        cT = sb("cT", [P, B, NQ], BF16)
        kTf = sb("kTf", [E0, NQ])
        sco = sb("sco", [P, QT, E1])
        scb = sb("scb", [P, QT, E1])
        two = sb("two", [P, QT * NG, 6])
        gin = sb("gin", [P, QT, 12])
        gm = sb("gm", [P, QT, NG])
        ein = sb("ein", [P, QT, 20])
        cw = sb("cw", [P, QT, E1])

        ps = [es.enter_context(nc.psum_tensor(f"ps{n}", [P, 512], F32)) for n in range(8)]

        s = {n: es.enter_context(nc.semaphore(n)) for n in (
            "ld_ctx ld_x ld_cf ld_cb ld_b ld_w0 ld_w1 ld_nat ld_kones zeros padded ones_row kst_free "
            "ctxT_ps ctxT_in pads k0_ps k0_f k0_hi k0_r k0_mid k0_r2 k0_lo k_wr k_st0 k_st1 k_st2 k_st3 a_oT a_oN c_pad k1_ps k1_lo k1_hi "
            "ctx4_in v_ps0 v_ps1 v0_in v1_in v_ones wt_ps wt_in "
            "q0_ps q0_f q0_hi q0_r q0_mid q0_r2 q0_lo q_wr q_st "
            "a_mp a_mx a_mT a_negm a_nm_st a_s a_exp a_pv a_rec a_nrm a_at a_ate a_op "
            "b_lg b_c b_sh b_ex b_mask b_pre b_loc b_keep b_kT b_kTb b_kTf b_bc b_mx b_mm b_bias b_yT b_y d_yT d_y "
            "c_q1 c_q1e c_qk c_mx c_sub c_tr c_exp c_pv c_rec c_nrm c_at c_ate c_op "
            "d_lg d_ex d_c d_c3 d_cTp d_cT d_up d_cb d_r d_g d_h d_dn out_wr "
            "xb0 xb2 r0 r1 r2 r3").split()}
        for k in range(4):
            for n in ("ln_st", "ln_ag", "ln_ve", "ln_rs", "ln_xn", "ln_xT", "ln_T"):
                s[f"{n}{k}"] = es.enter_context(nc.semaphore(f"{n}{k}"))
        s["ln_Tf1"] = es.enter_context(nc.semaphore("ln_Tf1"))
        s["ln_Tf3"] = es.enter_context(nc.semaphore("ln_Tf3"))

        def full(b, per, n, ring):
            return b * per + max(n + 1 - ring, 0)

        def phases(eng, first, step_a, step_b, step_c, step_d):
            first(0)
            with eng.Fori(1, B) as b:
                first(b)
            for new, old in ((0, None), (1, 0), (2, 1), (3, 2), (None, 3)):
                for i in range(QT):
                    step_a(new, old, i)
            for step in (step_b, step_c, step_d):
                for i in range(QT):
                    step(0, None, i)
                for i in range(QT):
                    step(1, 0, i)
                with eng.Fori(2, B) as b:
                    for i in range(QT):
                        step(b, b - 1, i)
                for i in range(QT):
                    step(None, B - 1, i)

        RESID = {1: ("r0", 1), 2: ("r1", QT), 3: ("r2", QT)}
        block = es.enter_context(nc.Block())

        @block.sync
        def _(sp):
            sp.dma_start(ctxa, ctx.rearrange("b k c -> k b c")[0:P]).then_inc(s["ld_ctx"], 16)
            sp.dma_start(ctxb, ctx.rearrange("b k c -> k b c")[P:NK]).then_inc(s["ld_ctx"], 16)
            sp.dma_start(cfs[:], cf).then_inc(s["ld_cf"], 16)
            sp.dma_start(xs[:], x.rearrange("b (t p) d -> p (b t) d", p=P)).then_inc(s["ld_x"], 16)
            for dst, src in ((bo0s, bo0), (bo1s, bo1), (biases, bias_e)):
                sp.dma_start(dst[:], src.partition_broadcast(P)).then_inc(s["ld_b"], 16)
            sp.dma_start(wq1s[:], wq1).then_inc(s["ld_w1"], 16)
            sp.dma_start(wk1s, wk1).then_inc(s["ld_w1"], 16)
            sp.dma_start(wv1s, wv1).then_inc(s["ld_w1"], 16)
            sp.dma_start(wo1s[:], wo1.rearrange("(c p) n -> p c n", p=P)).then_inc(s["ld_w1"], 16)
            for n, have in enumerate(("k0_hi", "k0_mid", "k0_lo")):
                sp.wait_ge(s[have], 1)
                sp.dma_start(kd[n], kp[:, n, :].rearrange("p (b k) -> p b k", b=B)).then_inc(s["k_wr"], 16)
            sp.wait_ge(s["zeros"], 1)
            sp.wait_ge(s["k_wr"], 48)
            def stack_keys(b):
                for t, (_, part) in enumerate(TERMS):
                    for a in range(2):
                        for odd in range(2):
                            at = (t * 2 + a) * HD0
                            o = odd * ODD + a * NK
                            src = kd[part].rearrange("(r o a d) b k -> o a d b r k", o=2, a=2, d=HD0)[odd, a]
                            sp.dma_start(kst[at:at + HD0, b, odd:PAIRS0:2, o:o + NK],
                                         src[:, b]).then_inc(s[f"k_st{b}"], 16)

            stack_keys(0)
            sp.dma_start(kst[KR:KM].rearrange("p b (r o) c -> p (b r) (o c)", o=2),
                         kones.bitcast(BF16).unsqueeze(1).broadcast_to([2, B * PAIRS0 // 2, 2 * PW])).then_inc(s["ld_kones"], 16)

            def first(b):
                for n, have in enumerate(("q0_hi", "q0_mid", "q0_lo")):
                    sp.wait_ge(s[have], b + 1)
                    sp.dma_start(qd[n][:, b, :], qp[:, n, :]).then_inc(s["q_wr"], 16)
                sp.wait_ge(s["q_wr"], 48 * b + 48)
                for t, (part, _) in enumerate(TERMS):
                    sp.dma_start(qst[16 * t:16 * t + 16, b, :, :],
                                 qd[part].rearrange("(r q) b n -> q b r n", q=16)[:, b]).then_inc(s["q_st"], 16)

            def step_a(new, old, i):
                if old is None and i == 0:
                    stack_keys(1)
                if new is not None and i == QT - 1:
                    sp.wait_ge(s["a_negm"], new + 1)
                    for a in range(2):
                        sp.dma_start(qst[KR + a:KR + a + 1, new, :, :],
                                     negm[a:H0:2, :]).then_inc(s["a_nm_st"], 16)
                    if new + 2 < B:
                        stack_keys(new + 2)

            def nothing(new, old, i):
                pass

            def step_d(new, old, i):
                if old is not None and i == QT - 1:
                    sp.wait_ge(s["r3"], old + 1)
                    sp.dma_start(out.rearrange("(b t p) d -> b p t d", b=B, p=P)[old],
                                 xs[:].rearrange("p (b t) d -> p b t d", b=B)[:, old]).then_inc(s["out_wr"], 16)

            phases(sp, first, step_a, nothing, nothing, step_d)
            sp.wait_ge(s["out_wr"], 16 * B)

        @block.gpsimd
        def _(pool):
            nc.gpsimd.memset(keys[0:KM, :].bitcast(U32), 0).then_inc(s["zeros"], 1)
            nc.gpsimd.memset(k1[:], 0.0).then_inc(s["padded"], 1)
            pool.wait_ge(s["ld_cf"], 16)

            def ln(k, b):
                pool.wait_ge(s[f"ln_ve{k}"], b + 1)
                nc.gpsimd.tensor_tensor(rstd[:, b, :], ve[:, b, :], minus_half, ALU.pow).then_inc(s[f"ln_rs{k}"], 1)

            def add_bias(k, b, bias, done):
                pool.wait_ge(s[f"ln_xn{k}"], QT * b + QT)
                xb = xs[:].rearrange("p (b t) d -> p b t d", b=B)[:, b]
                nc.gpsimd.tensor_tensor(xb, xb, bias[:].unsqueeze(1).broadcast_to([P, QT, D]), ALU.add)\
                    .then_inc(s[done], 1)

            pool.wait_ge(s["ld_b"], 48)

            def first(b):
                ln(0, b)
                pool.wait_ge(s["q0_hi"], b + 1)
                nc.gpsimd.tensor_tensor(qr, qf, qp[:, 0, :], ALU.subtract).then_inc(s["q0_r"], 1)
                pool.wait_ge(s["q0_mid"], b + 1)
                pool.wait_ge(s["q_wr"], 48 * b)
                nc.gpsimd.tensor_tensor(qp[:, 2, :], qr, qp[:, 1, :], ALU.subtract).then_inc(s["q0_lo"], 1)
                add_bias(0, b, bo0s, "xb0")

            def step_a(new, old, i):
                pass

            def step_b(new, old, i):
                if new is not None and i == 0:
                    ln(1, new)

            def step_c(new, old, i):
                if new is not None and i == 0:
                    ln(2, new)
                    add_bias(2, new, bo1s, "xb2")

            def step_d(new, old, i):
                if old is not None:
                    for j in ([0] if i == 0 else []) + ([i + 1] if i + 1 < QT else []):
                        for t in [t for t in UPS[j] if t < RT]:
                            pool.wait_ge(s["d_r"], HT * old + t + 1)
                            pool.wait_ge(s["d_dn"], HT * old)
                            pool.wait_ge(s["d_g"], RT * old + t + 1)
                            nc.gpsimd.tensor_tensor(hh[:, t, :], gg[:, t % 4, :], rr[:, t % 5, :], ALU.mult)\
                                .then_inc(s["d_h"], 1)
                if new is not None and i == 0:
                    ln(3, new)

            phases(pool, first, step_a, step_b, step_c, step_d)

        @block.scalar
        def _(act):
            for dst, src in ((wk0s[0:DC], wk0), (wk0s[DC:DC + 1], bk0.unsqueeze(0)), (wq0s[:], wq0),
                             (bq0s[:], bq0.unsqueeze(1)), (wv0s[0:DC], wv0), (wv0s[DC:DC + 1], bv0.unsqueeze(0)),
                             (wo0s[:], wo0)):
                act.dma_start(dst, src).then_inc(s["ld_w0"], 16)
            act.dma_start(cbs[:], cb.bitcast(BF16)).then_inc(s["ld_cb"], 16)
            for dst, src in ((wgs[:], wg), (bes[:], be), (nat_we, we.rearrange("e f h -> f e h")),
                             (nat_up, up_w.rearrange("(t u) i h -> (u i) t h", u=2)),
                             (nat_dn.rearrange("p t (u i) -> p t u i", u=2),
                              down_w.rearrange("(t u) d i -> d t u i", u=2)),
                             (nat_sup, sup_w.rearrange("(t p) h -> p t h", p=P)),
                             (nat_sdn, sdown_w.rearrange("d (t i) -> d t i", i=P)), (nat_gw, gate_w)):
                act.dma_start(dst, src).then_inc(s["ld_nat"], 16)
            for n in range(2):
                act.wait_ge(s["ctxT_ps"], n + 1)
                nc.scalar.activation(ctxT[0:DC, n * 2 * NK:(n + 1) * 2 * NK], ps[2 + n][0:DC, 0:2 * NK], ACT.Copy)\
                    .then_inc(s["ctxT_in"], 1)
            act.wait_ge(s["k0_f"], 2)
            nc.scalar.activation(kp[:, 0, :], kf, ACT.Copy).then_inc(s["k0_hi"], 1)
            act.wait_ge(s["k0_r"], 1)
            nc.scalar.activation(kp[:, 1, :], kr, ACT.Copy).then_inc(s["k0_mid"], 1)
            act.wait_ge(s["padded"], 1)
            for n in range(2 * PAIRS1):
                p, h = n // 2, n % 2
                act.wait_ge(s["k1_ps"], n + 1)
                nc.scalar.activation(k1[0:64, 2 * h:2 * h + 2, p, 0, :],
                                     ps[4 + n % 4][0:64, 0:2 * NK].rearrange("p (b k) -> p b k", b=2),
                                     ACT.Copy).then_inc(s["k1_lo"], 1)
            weights = [(weT[:, 0:4, :], 4), (weT[:, 4:8, :], 4), (upT[:, 0:4, :], 4), (upT[:, 4:8, :], 4),
                       (upT[:, 8:10, :], 2), (dnT[:, 0:4, :], 4), (dnT[:, 4:8, :], 4), (dnT[:, 8:10, :], 2)]
            for n, (dst, c) in enumerate(weights):
                act.wait_ge(s["wt_ps"], n + 1)
                nc.scalar.activation(dst, ps[2 + n % 2][:, 0:c * P].rearrange("p (t n) -> p t n", n=P), ACT.Copy)\
                    .then_inc(s["wt_in"], 1)
            act.wait_ge(s["wt_ps"], 9)
            nc.scalar.activation(gateT[:], ps[2][:, 0:E1], ACT.Copy).then_inc(s["wt_in"], 1)

            def lnT_out(k, b):
                act.wait_ge(s[f"ln_xT{k}"], b + 1)
                if k == 0:
                    act.wait_ge(s["q0_ps"], b)
                    nc.scalar.activation(lnTf[:], ps[0][:], ACT.Copy).then_inc(s["ln_T0"], 1)
                    return
                nc.scalar.activation(lnT[:, b, :], ps[0][:], ACT.Copy).then_inc(s[f"ln_T{k}"], 1)
                if k != 2:
                    act.wait_ge(s["b_lg" if k == 1 else "d_lg"], b)
                    nc.scalar.activation(lnTf[:], ps[0][:], ACT.Copy).then_inc(s[f"ln_Tf{k}"], 1)

            def first(b):
                lnT_out(0, b)
                act.wait_ge(s["q0_f"], b + 1)
                act.wait_ge(s["q_wr"], 48 * b)
                nc.scalar.activation(qp[:, 0, :], qf, ACT.Copy).then_inc(s["q0_hi"], 1)
                act.wait_ge(s["q0_r"], b + 1)
                nc.scalar.activation(qp[:, 1, :], qr, ACT.Copy).then_inc(s["q0_mid"], 1)
                act.wait_ge(s["v_ps1"], b + 1)
                for j in range(CH):
                    bank, at = ((6, 0), (6, 256), (7, 0), (7, 256), (6, 128))[j]
                    v = ps[bank][:, at:at + G1 * WIDE[j] * HD1].rearrange("p (g w d) -> p g w d", g=G1, w=WIDE[j])
                    for w in range(WIDE[j]):
                        nc.scalar.activation(v1[:, b, j, :, w, 0:HD1], v[:, :, w, :], ACT.Copy,
                                             scale=winmask[:, j, w:w + 1]).then_inc(s["v1_in"], 1)

            def step_a(new, old, i):
                if old is not None:
                    for n in range(CH * i, CH * i + CH):
                        act.wait_ge(s["a_s"], CH * 4 * old + n + 1)
                        act.wait_ge(s["a_pv"], full(old, CH * 4, n, 4))
                        nc.scalar.activation(pt0[:, n % 4, :], ps[4 + n % 2][:], ACT.Exp, scale=SCALE0)\
                            .then_inc(s["a_exp"], 1)
                    act.wait_ge(s["a_pv"], CH * (4 * old + i + 1))
                    act.wait_ge(s["a_oN"], 4 * old + i)
                    nc.scalar.activation(oT, ps[6 + i % 2][0:36, :], ACT.Copy).then_inc(s["a_oT"], 1)
                    if i == QT - 1:
                        act.wait_ge(s["a_at"], old + 1)
                        nc.scalar.activation(aoT0[:], ps[1][:], ACT.Copy).then_inc(s["a_ate"], 1)
                if new is not None and i == QT - 1:
                    act.wait_ge(s["a_mT"], new + 1)
                    act.wait_ge(s["a_nm_st"], 32 * new)
                    nc.scalar.activation(negm[:], ps[0][0:H0, :], ACT.Copy, scale=-1.0).then_inc(s["a_negm"], 1)

            def step_b(new, old, i):
                if old is not None and i == QT - 1:
                    act.wait_ge(s["b_mm"], E0 * old + E0)
                    act.wait_ge(s["b_y"], old)
                    nc.scalar.activation(yT, ps[6][:], ACT.Copy).then_inc(s["b_yT"], 1)
                if new is None:
                    return
                if i == 0:
                    lnT_out(1, new)
                if i == 1:
                    act.wait_ge(s["b_sh"], new + 1)
                    nc.scalar.activation(lex[:, :, 0:E0], lsh[:, :, 0:E0], ACT.Exp).then_inc(s["b_ex"], 1)
                if i == 3:
                    act.wait_ge(s["b_kT"], new + 1)
                    kt = ps[0][0:E0, 0:256].bitcast(BF16)
                    nc.scalar.activation(cT[:, new, :], ps[0][:, 0:256].bitcast(BF16), ACT.Copy).then_inc(s["b_kTb"], 1)
                    act.wait_ge(s["b_bias"], new)
                    nc.scalar.activation(kTf[:], kt, ACT.Copy).then_inc(s["b_kTf"], 1)

            def step_c(new, old, i):
                def q1_out(b, i):
                    act.wait_ge(s["c_q1"], QT * b + i + 1)
                    act.wait_ge(s["c_qk"], 16 * b + 4 * i)
                    nc.scalar.activation(q1T.rearrange("p r n -> p (r n)"), ps[0][:], ACT.Copy).then_inc(s["c_q1e"], 1)

                def exps(b, i):
                    for u in range(3):
                        n = 3 * i + u
                        c = 512 if u < 2 else 256
                        act.wait_ge(s["c_tr"], 12 * b + n + 1)
                        act.wait_ge(s["c_pv"], full(b, 2 * QT, 2 * i + 1, 4))
                        nc.scalar.activation(pt1[:, i % 2, 512 * u:512 * u + c], ps[4 + n % 2][:, 0:c], ACT.Exp,
                                             scale=SCALE1).then_inc(s["c_exp"], 1)

                if old is not None:
                    if i == 0:
                        q1_out(old, 0)
                        exps(old, 0)
                        q1_out(old, 1)
                    if i < QT - 1:
                        exps(old, i + 1)
                    act.wait_ge(s["c_at"], QT * old + i + 1)
                    nc.scalar.activation(aoT1.rearrange("p c n -> p (c n)"), ps[1][:], ACT.Copy).then_inc(s["c_ate"], 1)
                    if i < QT - 2:
                        q1_out(old, i + 2)
                if new is not None and i == 0:
                    lnT_out(2, new)

            def step_d(new, old, i):
                if old is not None:
                    for j in ([0] if i == 0 else []) + ([i + 1] if i + 1 < QT else []):
                        for t in UPS[j]:
                            act.wait_ge(s["d_up"], HT * old + t + 1)
                            act.wait_ge(s["d_h"], full(old, HT, t, 5))
                            nc.scalar.activation(rr[:, t % 5, :], ps[2 + t % 2][:], ACT.Relu).then_inc(s["d_r"], 1)
                        for t in [t for t in UPS[j] if t >= RT]:
                            act.wait_ge(s["d_r"], HT * old + t + 1)
                            act.wait_ge(s["d_dn"], HT * old)
                            act.wait_ge(s["d_h"], HT * old + t)
                            nc.scalar.activation(hh[:, t, :], rr[:, t % 5, :], ACT.Square).then_inc(s["d_h"], 1)
                if old is not None and i == QT - 1:
                    act.wait_ge(s["d_dn"], HT * old + HT)
                    act.wait_ge(s["d_y"], old)
                    nc.scalar.activation(yT, ps[6][:], ACT.Copy).then_inc(s["d_yT"], 1)
                if new is not None:
                    if i == 0:
                        lnT_out(3, new)
                    if i == 1:
                        act.wait_ge(s["d_lg"], new + 1)
                        nc.scalar.activation(lex[:].rearrange("p t e -> p (t e)"), ps[0][:, 0:QT * E1], ACT.Exp,
                                             scale=-1.0).then_inc(s["d_ex"], 1)
                    if i == 3:
                        act.wait_ge(s["d_cTp"], new + 1)
                        nc.scalar.activation(cT[:, new, :], ps[0][:, 0:256].bitcast(BF16), ACT.Copy)\
                            .then_inc(s["d_cT"], 1)

            phases(act, first, step_a, step_b, step_c, step_d)

        @block.tensor
        def _(pe):
            mm = nc.tensor.matmul
            pe.wait_ge(s["ld_ctx"], 32)
            pe.wait_ge(s["ld_cf"], 16)
            for b in range(B):
                o = b % 2 * NK
                nc.tensor.transpose(ps[2 + b // 2][0:DC, o:o + P], ctxa[:, b, :], ident)
                last = nc.tensor.transpose(ps[2 + b // 2][0:DC, o + P:o + NK], ctxb[:, b, :], ident[0:NK - P, 0:NK - P])
                if b % 2:
                    last.then_inc(s["ctxT_ps"], 1)
            pe.wait_ge(s["ctxT_in"], 2)
            pe.wait_ge(s["ones_row"], 1)
            pe.wait_ge(s["ld_w0"], 112)
            for n in range(2):
                mm(ps[4 + n][:, 0:2 * NK], wk0s, ctxT[:, n * 2 * NK:(n + 1) * 2 * NK], start=True, stop=True)\
                    .then_inc(s["k0_ps"], 1)
            pe.wait_ge(s["ld_w1"], 64)
            pe.wait_ge(s["k0_f"], 2)
            for n in range(2 * PAIRS1):
                p, h = n // 2, n % 2
                if n >= 4:
                    pe.wait_ge(s["k1_lo"], n - 3)
                    pe.wait_ge(s["k1_hi"], n - 3)
                mm(ps[4 + n % 4][:, 0:2 * NK], wk1s[:, p * P:(p + 1) * P],
                   ctxT[0:DC, h * 2 * NK:(h + 1) * 2 * NK], start=True, stop=True).then_inc(s["k1_ps"], 1)
            pe.wait_ge(s["ld_nat"], 128)
            blocks_of = ([[nat_we[:, 4 * n + e, :] for e in range(4)] for n in range(2)]
                   + [[nat_up[:, 4 * n + e, :] for e in range(4)] for n in range(2)]
                   + [[nat_sup[:, e, :] for e in range(2)]]
                   + [[nat_dn[:, 4 * n + e, :] for e in range(4)] for n in range(2)]
                   + [[nat_sdn[:, e, :] for e in range(2)]])
            for n, blocks in enumerate(blocks_of):
                if n >= 2:
                    pe.wait_ge(s["wt_in"], n - 1)
                for e, w in enumerate(blocks):
                    last = nc.tensor.transpose(ps[2 + n % 2][:, e * P:(e + 1) * P], w, ident)
                last.then_inc(s["wt_ps"], 1)
            pe.wait_ge(s["wt_in"], 7)
            nc.tensor.transpose(ps[2][:, 0:E1], nat_gw, ident[0:E1, 0:E1]).then_inc(s["wt_ps"], 1)
            pe.wait_ge(s["k1_lo"], 8)
            pe.wait_ge(s["k1_hi"], 8)
            pe.wait_ge(s["ld_cb"], 16)

            def ln(k, b):
                for i in range(QT):
                    pe.wait_ge(s[f"ln_xn{k}"], QT * b + i + 1)
                    last = nc.tensor.transpose(ps[0][:, i * P:(i + 1) * P], xn[:, i, :], ident)
                last.then_inc(s[f"ln_xT{k}"], 1)

            def first(b):
                pe.wait_ge(s["ln_T0"], b)
                ln(0, b)
                pe.wait_ge(s["ln_T0"], b + 1)
                pe.wait_ge(s["q0_f"], b)
                mm(ps[1][:], wq0s[:], lnTf[:], start=True, stop=True).then_inc(s["q0_ps"], 1)
                pe.wait_ge(s["ctx4_in"], b + 1)
                pe.wait_ge(s["v0_in"], CH * b)
                for j in range(CH):
                    last = mm(ps[4 + j // 4][:, j % 4 * P:j % 4 * P + P], ctx4[:, j * P:(j + 1) * P], wv0s,
                              start=True, stop=True)
                last.then_inc(s["v_ps0"], 1)
                pe.wait_ge(s["v1_in"], 8 * b)
                for j in (0, 4, 1, 2, 3):
                    bank, at = ((6, 0), (6, 256), (7, 0), (7, 256), (6, 128))[j]
                    n = WIDE[j] * HD1
                    rhs = wv1s.rearrange("p (g c) -> p g c", g=G1)[:, :, FIRST[j] * HD1:FIRST[j] * HD1 + n]
                    last = mm(ps[bank][:, at:at + G1 * n].rearrange("p (g c) -> p g c", g=G1),
                              ctx4[0:DC, j * P:(j + 1) * P], rhs, start=True, stop=True)
                last.then_inc(s["v_ps1"], 1)

            PARTS = [[(0, 0)], [(0, P)], [(0, 2 * P), (1, 0)], [(1, P)], [(1, 2 * P)]]

            def step_a(new, old, i):
                def maxima(p):
                    n = PAIRS0 * i + p
                    o = p % 2 * ODD
                    pe.wait_ge(s["a_mx"], full(new, PAIRS0 * QT, n, 2))
                    mm(ps[2 + p % 2][:, 0:2 * NK], qst[0:KR, new, p, i * P:(i + 1) * P],
                       kst[0:KR, new, p, o:o + 2 * NK], start=True, stop=True).then_inc(s["a_mp"], 1)

                def scores(j):
                    n = CH * i + j
                    pe.wait_ge(s["a_exp"], full(old, CH * 4, n, 2))
                    for q, (e, c) in enumerate(PARTS[j]):
                        last = mm(ps[4 + n % 2][:], kst[:, old, 2 * i + e, c:c + P], qst[:, old, 2 * i + e, :],
                                  start=(q == 0), stop=(q == len(PARTS[j]) - 1))
                    last.then_inc(s["a_s"], 1)

                def values(j):
                    n = CH * i + j
                    pe.wait_ge(s["a_exp"], CH * 4 * old + n + 1)
                    if j == 0:
                        pe.wait_ge(s["a_oT"], full(old, 4, i, 2))
                    mm(ps[6 + i % 2][0:36, :], v0[:, old, j, i].rearrange("p a d -> p (a d)"), pt0[:, n % 4, :],
                       start=(j == 0), stop=(j == CH - 1)).then_inc(s["a_pv"], 1)

                if new is not None and i == 0:
                    pe.wait_ge(s["q_st"], 96 * new + 96)
                    pe.wait_ge(s[f"k_st{new}"], 16 * 24)
                    if old is None:
                        pe.wait_ge(s["wt_in"], 9)
                        pe.wait_ge(s["ln_T0"], B)
                        pe.wait_ge(s["q0_f"], B)
                        pe.wait_ge(s["v0_in"], CH * B)
                        pe.wait_ge(s["v1_in"], 8 * B)
                if old is not None and i == 0:
                    pe.wait_ge(s["a_nm_st"], 32 * old + 32)
                    pe.wait_ge(s["ld_kones"], 16)
                    pe.wait_ge(s["v_ones"], B)
                order = [[0, 1], [2, 3], [4, 5], [6], [7]]
                if old is not None:
                    scores(0)
                    scores(1)
                for j in range(CH):
                    if new is not None:
                        for p in order[j]:
                            maxima(p)
                    if old is not None:
                        values(j)
                        if j + 2 < CH:
                            scores(j + 2)
                if old is not None:
                    pe.wait_ge(s["a_oT"], 4 * old + i + 1)
                    pe.wait_ge(s["a_nrm"], 4 * old + i)
                    pe.wait_ge(s["r0"], old)
                    for q in range(QT):
                        last = nc.tensor.transpose(ps[1][:, 36 * q:36 * q + 36], oT[:, q * P:(q + 1) * P],
                                                   ident[0:36, 0:36])
                    last.then_inc(s["a_oN"], 1)
                if i == QT - 1:
                    if old is not None:
                        pe.wait_ge(s["a_nrm"], 4 * old + 4)
                        pe.wait_ge(s["r0"], old)
                        for q in range(QT):
                            last = nc.tensor.transpose(ps[1][:, q * P:(q + 1) * P], ao0[:, q, :], ident)
                        last.then_inc(s["a_at"], 1)
                    if new is not None:
                        pe.wait_ge(s["a_mx"], PAIRS0 * QT * (new + 1))
                        pe.wait_ge(s["a_negm"], new)
                        for q in range(QT):
                            last = nc.tensor.transpose(ps[0][0:H0, q * P:(q + 1) * P], mx[:, q, :], ident)
                        last.then_inc(s["a_mT"], 1)
                    if old is not None:
                        pe.wait_ge(s["a_ate"], old + 1)
                        for q in range(QT):
                            last = mm(ps[1][:, q * P:(q + 1) * P], aoT0[:, q * P:(q + 1) * P], wo0s[:],
                                      start=True, stop=True)
                        last.then_inc(s["a_op"], 1)

            def step_b(new, old, i):
                def spread(e):
                    pe.wait_ge(s["b_mx"], full(old, E0, e, 2))
                    mm(ps[4 + e % 2][:], sel8[:, e, :], cT[:, old, :], start=True, stop=True).then_inc(s["b_bc"], 1)

                if old is not None:
                    if i == 0:
                        pe.wait_ge(s["b_kTb"], old + 1)
                        spread(0)
                        spread(1)
                        pe.wait_ge(s["b_kTf"], old + 1)
                        pe.wait_ge(s["b_yT"], old)
                        mm(ps[6][:], bes[:], kTf[:], start=True, stop=False).then_inc(s["b_bias"], 1)
                    if i < QT - 1:
                        spread(2 * i + 2)
                        spread(2 * i + 3)
                    for e in (2 * i, 2 * i + 1):
                        pe.wait_ge(s["b_mx"], E0 * old + e + 1)
                        mm(ps[6][:], weT[:, e, :], mxr[:, e % 4, :], start=False, stop=(e == E0 - 1))\
                            .then_inc(s["b_mm"], 1)
                    if i == QT - 1:
                        pe.wait_ge(s["b_yT"], old + 1)
                        pe.wait_ge(s["r1"], QT * old)
                        for q in range(QT):
                            last = nc.tensor.transpose(ps[7][:, q * P:(q + 1) * P], yT[:, q * P:(q + 1) * P], ident)
                        last.then_inc(s["b_y"], 1)
                if new is not None:
                    if i == 0:
                        if old is None:
                            pe.wait_ge(s["r0"], B)
                            pe.wait_ge(s["a_negm"], B)
                        pe.wait_ge(s["b_kTf"], new)
                        ln(1, new)
                    if i == 1:
                        pe.wait_ge(s["ln_Tf1"], new + 1)
                        for q in range(QT):
                            last = mm(ps[0][:, q * E0:(q + 1) * E0], lnTf[:, q * P:(q + 1) * P], wgs[:],
                                      start=True, stop=True)
                        last.then_inc(s["b_lg"], 1)
                    if i == 2:
                        pe.wait_ge(s["b_mask"], new + 1)
                        mm(ps[0][:, 0:QT * E0], before, mk[:].rearrange("p t e -> p (t e)"),
                           start=True, stop=False, skip_group_check=True)
                        for q in range(QT):
                            last = mm(ps[0][:, (q + 1) * E0:(QT + 1) * E0].rearrange("p (t e) -> p t e", e=E0),
                                      onesb, mk[:, q:q + 1, :].broadcast_to([P, QT - q, E0]),
                                      start=False, stop=(q == QT - 1), skip_group_check=True)
                        last.then_inc(s["b_pre"], 1)
                    if i == 3:
                        pe.wait_ge(s["b_keep"], new + 1)
                        for q in range(QT):
                            last = nc.tensor.transpose(ps[0][:, 64 * q:64 * q + 64].bitcast(BF16), part[:, q, :], identb)
                        last.then_inc(s["b_kT"], 1)

            def step_c(new, old, i):
                def queries(b, i):
                    pe.wait_ge(s["ln_T2"], b + 1)
                    pe.wait_ge(s["c_q1e"], QT * b + i)
                    for p in range(PAIRS1):
                        last = mm(ps[0][:, p * P:(p + 1) * P], wq1s[:, p * P:(p + 1) * P],
                                  lnT[:, b, i * P:(i + 1) * P], start=True, stop=True)
                    last.then_inc(s["c_q1"], 1)

                def scores(b, i):
                    pe.wait_ge(s["c_q1e"], QT * b + i + 1)
                    for p in range(PAIRS1):
                        n = PAIRS1 * i + p
                        pe.wait_ge(s["c_sub"], full(b, 16, n, 2))
                        mm(ps[2 + p % 2][:, 0:2 * NK], q1T[:, p, :], k1[:, b, p].rearrange("p a k -> p (a k)"),
                           start=True, stop=True).then_inc(s["c_qk"], 1)

                def turn(b, i):
                    pe.wait_ge(s["c_sub"], 16 * b + 4 * i + 4)
                    for u in range(3):
                        n = 3 * i + u
                        pe.wait_ge(s["c_exp"], full(b, 12, n, 2))
                        for c in range(4 if u < 2 else 2):
                            last = nc.tensor.transpose(ps[4 + n % 2][:, c * P:(c + 1) * P],
                                                       s1[:, i % 2, (4 * u + c) * P:(4 * u + c + 1) * P], ident)
                        last.then_inc(s["c_tr"], 1)

                def values(b, i):
                    for g in range(G1):
                        pe.wait_ge(s["c_nrm"], full(b, 2 * QT, 2 * i + g, 2))
                        for j in range(CH):
                            c = CH * g + j
                            pe.wait_ge(s["c_exp"], 12 * b + 3 * i + c // 4 + 1)
                            f, w = FIRST[j], WIDE[j]
                            last = mm(ps[6 + g][:, f * 65:(f + w) * 65], pt1[:, i % 2, c * P:(c + 1) * P],
                                      v1[:, b, j, g, 0:w, :].rearrange("p w d -> p (w d)"),
                                      start=(j == 0), stop=(j == CH - 1), skip_group_check=True)
                        last.then_inc(s["c_pv"], 1)

                if old is not None:
                    if i == 0:
                        pe.wait_ge(s["c_pad"], 1)
                        queries(old, 0)
                        scores(old, 0)
                        turn(old, 0)
                        queries(old, 1)
                    if i < QT - 1:
                        scores(old, i + 1)
                    values(old, i)
                    if i < QT - 1:
                        turn(old, i + 1)
                    pe.wait_ge(s["c_nrm"], 2 * QT * old + 2 * i + 2)
                    pe.wait_ge(s["r2"], QT * old + i)
                    for c in range(4):
                        last = nc.tensor.transpose(ps[1][:, c * P:(c + 1) * P], ao1[:, c * P:(c + 1) * P], ident)
                    last.then_inc(s["c_at"], 1)
                    if i < QT - 2:
                        queries(old, i + 2)
                    pe.wait_ge(s["c_ate"], QT * old + i + 1)
                    for c in range(4):
                        last = mm(ps[1][:, 0:D], aoT1[:, c, :], wo1s[:, c, :], start=(c == 0), stop=(c == 3))
                    last.then_inc(s["c_op"], 1)
                if new is not None and i == 0:
                    if old is None:
                        pe.wait_ge(s["r1"], QT * B)
                    else:
                        pe.wait_ge(s["c_q1e"], QT * old + 3)
                    ln(2, new)
                if new is not None and old is not None and i == 0:
                    pe.wait_ge(s["ln_T2"], new + 1)

            def step_d(new, old, i):
                def up(t):
                    pe.wait_ge(s["d_r"], full(old, HT, t, 2))
                    mm(ps[2 + t % 2][:], upT[:, t, :], lnT[:, old, :], start=True, stop=True).then_inc(s["d_up"], 1)
                    if t < RT:
                        pe.wait_ge(s["d_g"], full(old, RT, t, 2))
                        mm(ps[4 + t % 2][:], sel48[:, t, :], cT[:, old, :], start=True, stop=True).then_inc(s["d_cb"], 1)

                if old is not None:
                    if i == 0:
                        pe.wait_ge(s["d_cT"], old + 1)
                        for t in UPS[0]:
                            up(t)
                        pe.wait_ge(s["d_yT"], old)
                    if i < QT - 1:
                        for t in UPS[i + 1]:
                            up(t)
                    for t in UPS[i]:
                        pe.wait_ge(s["d_h"], HT * old + t + 1)
                        mm(ps[6][:], dnT[:, t, :], hh[:, t, :], start=(t == 0), stop=(t == HT - 1))\
                            .then_inc(s["d_dn"], 1)
                    if i == QT - 1:
                        pe.wait_ge(s["d_yT"], old + 1)
                        pe.wait_ge(s["r3"], old)
                        for q in range(QT):
                            last = nc.tensor.transpose(ps[7][:, q * P:(q + 1) * P], yT[:, q * P:(q + 1) * P], ident)
                        last.then_inc(s["d_y"], 1)
                if new is not None:
                    if i == 0:
                        if old is None:
                            pe.wait_ge(s["r2"], QT * B)
                        pe.wait_ge(s["d_cT"], new)
                        ln(3, new)
                    if i == 1:
                        pe.wait_ge(s["ln_Tf3"], new + 1)
                        for q in range(QT):
                            last = mm(ps[0][:, q * E1:(q + 1) * E1], lnTf[:, q * P:(q + 1) * P], gateT[:],
                                      start=True, stop=True)
                        last.then_inc(s["d_lg"], 1)
                    if i == 3:
                        pe.wait_ge(s["d_c3"], new + 1)
                        for q in range(QT):
                            last = nc.tensor.transpose(ps[0][:, 64 * q:64 * q + 64].bitcast(BF16), part[:, q, :], identb)
                        last.then_inc(s["d_cTp"], 1)

            phases(pe, first, step_a, step_b, step_c, step_d)

        @block.vector
        def _(dve):
            tt, ts, stt = nc.vector.tensor_tensor, nc.vector.tensor_scalar, nc.vector.scalar_tensor_tensor
            v = nc.vector

            class Chain:
                def __init__(self, name, base, per):
                    self.sem, self.base, self.per, self.n = s[name], base * per, per, 0

                def __call__(self, ins):
                    self.n += 1
                    ins.then_inc(self.sem, 1)
                    dve.wait_ge(self.sem, self.base + self.n)

                def add(self, ins):
                    self.n += 1
                    ins.then_inc(self.sem, 1)

                def wait(self):
                    dve.wait_ge(self.sem, self.base + self.n)

                def hold(self):
                    self.add(v.memset(tick[:, 1:2], 0.0))

            v.memset(ctxT[DC:DC + 1, :], 1.0).then_inc(s["ones_row"], 1)
            v.memset(ctx4[:, ROWS:CH * P], 0.0)
            v.memset(part[:], 0.0)
            v.memset(pin[:], PAD)
            v.memset(gin[:], PAD)
            v.memset(ein[:], PAD)
            v.memset(carry[:, 0, :], 0.0).then_inc(s["pads"], 1)
            for n in range(2):
                dve.wait_ge(s["k0_ps"], n + 1)
                v.tensor_copy(kf[:, n * 2 * NK:(n + 1) * 2 * NK], ps[4 + n][:, 0:2 * NK]).then_inc(s["k0_f"], 1)
            dve.wait_ge(s["k0_hi"], 1)
            tt(kr, kf, kp[:, 0, :], ALU.subtract).then_inc(s["k0_r"], 1)
            dve.wait_ge(s["k0_mid"], 1)
            tt(kp[:, 2, :], kr, kp[:, 1, :], ALU.subtract).then_inc(s["k0_lo"], 1)
            dve.wait_ge(s["padded"], 1)
            for n in range(2 * PAIRS1):
                p, h = n // 2, n % 2
                dve.wait_ge(s["k1_ps"], n + 1)
                v.tensor_copy(k1[64:P, 2 * h:2 * h + 2, p, 1, :],
                              ps[4 + n % 4][64:P, 0:2 * NK].rearrange("p (b k) -> p b k", b=2)).then_inc(s["k1_hi"], 1)
            dve.wait_ge(s["ld_cf"], 16)
            for b in range(B):
                v.tensor_copy(v0[:, b, :, :, :, HD0], headmask.unsqueeze(2).broadcast_to([P, CH, 4, GH]))
                v.tensor_copy(v1[:, b, :, :, :, HD1], winmask.unsqueeze(2).broadcast_to([P, CH, G1, 2]))\
                    .then_inc(s["v_ones"], 1)
            dve.wait_ge(s["ld_x"], 16)
            dve.wait_ge(s["ctxT_in"], 2)
            dve.wait_ge(s["ones_row"], 1)
            dve.wait_ge(s["ld_w0"], 112)
            dve.wait_ge(s["ld_b"], 48)

            dve.wait_ge(s["pads"], 1)

            def ln(k, b):
                xb = xs[:].rearrange("p (b t) d -> p b t d", b=B)[:, b]
                if k:
                    name, per = RESID[k]
                    dve.wait_ge(s[name], per * b + per)
                dve.wait_ge(s[f"ln_xn{k}"], QT * b)
                if k and isinstance(b, int) and b == 0:
                    dve.wait_ge(s[f"ln_xn{k - 1}"], QT * B)
                    dve.wait_ge(s[f"ln_xT{k - 1}"], B)
                for i in range(QT):
                    v.bn_stats(st[:, i, :], xb[:, i, :]).then_inc(s[f"ln_st{k}"], 1)
                dve.wait_ge(s[f"ln_st{k}"], QT * b + QT)
                v.memset(tick[:, 0:1], 0.0).then_inc(s[f"ln_ag{k}"], 1)
                for i in range(QT):
                    v.bn_aggr(mv[:, i, :], st[:, i, :]).then_inc(s[f"ln_ag{k}"], 1)
                dve.wait_ge(s[f"ln_ag{k}"], (QT + 1) * b + QT + 1)
                ts(ve[:, b, :], mv[:, :, 1], EPS, None, ALU.add).then_inc(s[f"ln_ve{k}"], 1)
                dve.wait_ge(s[f"ln_rs{k}"], b + 1)
                dve.wait_ge(s[f"ln_xT{k}"], b)
                for i in range(QT):
                    ts(xn[:, i, :], xb[:, i, :], mv[:, i, 0:1], rstd[:, b, i:i + 1], ALU.subtract, ALU.mult)\
                        .then_inc(s[f"ln_xn{k}"], 1)

            def first(b):
                ln(0, b)
                dve.wait_ge(s["v_ps1"], b)
                v.tensor_copy(ctx4[:, 0:ROWS].rearrange("p (a k) -> p a k", a=GH),
                              ctxT[:].rearrange("p (b k) -> p b k", b=B)[:, b].unsqueeze(1)
                              .broadcast_to([DC + 1, GH, NK])).then_inc(s["ctx4_in"], 1)
                dve.wait_ge(s["q0_ps"], b + 1)
                dve.wait_ge(s["q0_r"], b)
                dve.wait_ge(s["q0_hi"], b)
                ts(qf, ps[1][:], bq0s[:], None, ALU.add).then_inc(s["q0_f"], 1)
                dve.wait_ge(s["v_ps0"], b + 1)
                for j in range(CH):
                    src = ps[4 + j // 4][:, j % 4 * P:j % 4 * P + P]
                    tt(v0[:, b, j, :, :, 0:HD0], src.rearrange("p (g a d) -> p g a d", g=4, a=GH),
                       headmask[:, j, :].unsqueeze(1).unsqueeze(3).broadcast_to([P, 4, GH, HD0]), ALU.mult)\
                        .then_inc(s["v0_in"], 1)

            def step_a(new, old, i):
                if new is not None:
                    for p in range(PAIRS0):
                        dve.wait_ge(s["a_mp"], PAIRS0 * QT * new + PAIRS0 * i + p + 1)
                        if p == 0 and i == 0:
                            dve.wait_ge(s["a_mT"], new)
                        v.reduce_max(mx[:, i, 2 * p:2 * p + 2],
                                     ps[2 + p % 2][:, 0:2 * NK].rearrange("p (a k) -> p a k", a=2), AX)\
                            .then_inc(s["a_mx"], 1)
                if old is not None:
                    dve.wait_ge(s["a_oN"], 4 * old + i + 1)
                    o = ps[1][:, 0:QT * 36].rearrange("p (q a d) -> p q a d", q=QT, a=GH)
                    dve.wait_ge(s["a_nrm"], 4 * old + i)
                    v.reciprocal(rec0[:], o[:, :, :, HD0]).then_inc(s["a_rec"], 1)
                    dve.wait_ge(s["a_rec"], 4 * old + i + 1)
                    dve.wait_ge(s["a_at"], old)
                    tt(ao0[:].rearrange("p q (g a d) -> p q g a d", g=4, a=GH)[:, :, i], o[:, :, :, 0:HD0],
                       rec0[:].unsqueeze(3).broadcast_to([P, QT, GH, HD0]), ALU.mult).then_inc(s["a_nrm"], 1)
                    if i == QT - 1:
                        dve.wait_ge(s["a_op"], old + 1)
                        dve.wait_ge(s["xb0"], old + 1)
                        xb = xs[:].rearrange("p (b t) d -> p b (t d)", b=B)[:, old]
                        tt(xb, ps[1][:], xb, ALU.add).then_inc(s["r0"], 1)

            def step_b(new, old, i):
                if old is not None:
                    for j in ([0] if i == 0 else []) + ([i + 1] if i + 1 < QT else []):
                        for e in (2 * j, 2 * j + 1):
                            dve.wait_ge(s["b_bc"], E0 * old + e + 1)
                            dve.wait_ge(s["b_mm"], full(old, E0, e, 4))
                            tt(mxr[:, e % 4, :], ps[4 + e % 2][:], lnT[:, old, :], ALU.mult).then_inc(s["b_mx"], 1)
                    if i == QT - 1:
                        dve.wait_ge(s["b_y"], old + 1)
                        xb = xs[:].rearrange("p (b t) d -> p b t d", b=B)[:, old]
                        for q in range(QT):
                            stt(xb[:, q, :], ps[7][:, q * P:(q + 1) * P], gate[:, old, q:q + 1], xb[:, q, :],
                                ALU.mult, ALU.add).then_inc(s["r1"], 1)
                if new is None:
                    return
                if i == 0:
                    ln(1, new)
                if i == 1:
                    c = Chain("b_c", new, 16)
                    dve.wait_ge(s["b_lg"], new + 1)
                    lg = ps[0][:, 0:QT * E0].rearrange("p (t e) -> p t e", e=E0)
                    c(v.reduce_max(col[:], lg, AX))
                    tt(lsh[:, :, 0:E0], lg, col[:].unsqueeze(2).broadcast_to([P, QT, E0]), ALU.subtract)\
                        .then_inc(s["b_sh"], 1)
                    dve.wait_ge(s["b_ex"], new + 1)
                    c(v.tensor_reduce(col[:], lex[:, :, 0:E0], AX, ALU.add))
                    c(v.reciprocal(col2[:], col[:]))
                    c(tt(pin[:, :, 0:E0], lex[:, :, 0:E0], col2[:].unsqueeze(2).broadcast_to([P, QT, E0]), ALU.mult))
                    c.hold()
                    for q in range(QT):
                        c.add(v.max(top[:, q, :], pin[:, q, 0:E0]))
                    c.wait()
                    c(v.tensor_copy(gate[:, new, :], top[:, :, 0]))
                    c(v.memset(top[:, :, 1:8], PAD))
                    c.hold()
                    for q in range(QT):
                        c.add(v.match_replace(pout[:, q, :], top[:, q, :], pin[:, q, :], HIT))
                    c.wait()
                    ts(mk[:], pout[:, :, 0:E0], HIT, None, ALU.is_equal).then_inc(s["b_mask"], 1)
                    assert c.n == c.per
                if i == 2:
                    dve.wait_ge(s["b_pre"], new + 1)
                    pre = ps[0][:, 0:(QT + 1) * E0].rearrange("p (t e) -> p t e", e=E0)
                    tt(loc[:], pre[:, 0:QT, :], carry[:, new, :].unsqueeze(1).broadcast_to([P, QT, E0]), ALU.add)\
                        .then_inc(s["b_loc"], 1)
                    tt(carry[:, new + 1, :], pre[:, QT, :], carry[:, new, :], ALU.add).then_inc(s["b_loc"], 1)
                    dve.wait_ge(s["b_loc"], 2 * new + 2)
                    stt(km, loc[:], float(CAP), mk[:], ALU.is_lt, ALU.mult).then_inc(s["b_keep"], 1)

            def step_c(new, old, i):
                def shift(b, i):
                    for p in range(PAIRS1):
                        n = PAIRS1 * i + p
                        dve.wait_ge(s["c_qk"], 16 * b + n + 1)
                        raw = ps[2 + p % 2][:, 0:2 * NK].rearrange("p (a k) -> p a k", a=2)
                        dve.wait_ge(s["c_sub"], full(b, 16, n, 4))
                        v.reduce_max(mx1[:, p, :], raw, AX).then_inc(s["c_mx"], 1)
                        dve.wait_ge(s["c_mx"], 16 * b + n + 1)
                        dve.wait_ge(s["c_tr"], full(b, 12, 3 * i + 2, 6))
                        at = p // 2 * CH * P + p % 2 * 2 * NK
                        tt(s1[:, i % 2, at:at + 2 * NK].rearrange("p (a k) -> p a k", a=2), raw,
                           mx1[:, p, :].unsqueeze(2).broadcast_to([P, 2, NK]), ALU.subtract).then_inc(s["c_sub"], 1)

                if i == 0 and old is None:
                    v.memset(s1.rearrange("p t (g c) -> p t g c", g=G1)[:, :, :, ROWS:CH * P], 0.0)\
                        .then_inc(s["c_pad"], 1)
                if old is not None:
                    if i == 0:
                        shift(old, 0)
                    if i < QT - 1:
                        shift(old, i + 1)
                    for g in range(G1):
                        dve.wait_ge(s["c_pv"], 2 * QT * old + 2 * i + g + 1)
                        o = ps[6 + g][:, 0:GH * 65].rearrange("p (a d) -> p a d", a=GH)
                        dve.wait_ge(s["c_nrm"], full(old, 2 * QT, 2 * i + g, 2))
                        v.reciprocal(rec1[:, g, :], o[:, :, HD1]).then_inc(s["c_rec"], 1)
                        dve.wait_ge(s["c_rec"], 2 * QT * old + 2 * i + g + 1)
                        dve.wait_ge(s["c_at"], QT * old + i)
                        tt(ao1[:, 256 * g:256 * g + 256].rearrange("p (a d) -> p a d", a=GH), o[:, :, 0:HD1],
                           rec1[:, g, :].unsqueeze(2).broadcast_to([P, GH, HD1]), ALU.mult).then_inc(s["c_nrm"], 1)
                    dve.wait_ge(s["c_op"], QT * old + i + 1)
                    dve.wait_ge(s["xb2"], old + 1)
                    xb = xs[:].rearrange("p (b t) d -> p b t d", b=B)[:, old, i]
                    tt(xb, ps[1][:, 0:D], xb, ALU.add).then_inc(s["r2"], 1)
                if new is not None and i == 0:
                    ln(2, new)

            def step_d(new, old, i):
                if old is not None:
                    for j in ([0] if i == 0 else []) + ([i + 1] if i + 1 < QT else []):
                        for t in UPS[j]:
                            if t < RT:
                                dve.wait_ge(s["d_r"], HT * old + t + 1)
                                dve.wait_ge(s["d_cb"], RT * old + t + 1)
                                dve.wait_ge(s["d_h"], HT * old + max(t - 3, 0))
                                tt(gg[:, t % 4, :], ps[4 + t % 2][:], rr[:, t % 5, :], ALU.mult).then_inc(s["d_g"], 1)
                    if i == QT - 1:
                        dve.wait_ge(s["d_y"], old + 1)
                        xb = xs[:].rearrange("p (b t) d -> p b (t d)", b=B)[:, old]
                        tt(xb, ps[7][:], xb, ALU.add).then_inc(s["r3"], 1)
                if new is None:
                    return
                if i == 0:
                    ln(3, new)
                if i == 1:
                    c = Chain("d_c", new, 41)
                    dve.wait_ge(s["d_ex"], new + 1)
                    c(ts(lex[:], lex[:], 1.0, None, ALU.add))
                    c(v.reciprocal(sco[:], lex[:]))
                    c(tt(scb[:], sco[:], biases[:].unsqueeze(1).broadcast_to([P, QT, E1]), ALU.add))
                    sg = scb[:].rearrange("p t (g e) -> p (t g) e", g=NG)
                    c(tt(two[:, :, 0:3], sg[:, :, 0:3], sg[:, :, 1:4], ALU.add))
                    c(tt(two[:, :, 3:5], sg[:, :, 0:2], sg[:, :, 2:4], ALU.add))
                    c(tt(two[:, :, 5:6], sg[:, :, 0:1], sg[:, :, 3:4], ALU.add))
                    c(v.reduce_max(gin[:, :, 0:NG], two[:].rearrange("p (t g) s -> p t g s", g=NG), AX))
                    c.hold()
                    for q in range(QT):
                        c.add(v.max(top[:, q, :], gin[:, q, :]))
                    c.wait()
                    c(v.memset(top[:, :, 2:8], PAD))
                    c.hold()
                    for q in range(QT):
                        c.add(v.match_replace(gout[:, q, :], top[:, q, :], gin[:, q, :], HIT))
                    c.wait()
                    c(ts(gm[:], gout[:, :, 0:NG], HIT, None, ALU.is_equal))
                    c(tt(cw[:].rearrange("p t (g e) -> p t g e", g=NG), scb[:].rearrange("p t (g e) -> p t g e", g=NG),
                         gm[:].unsqueeze(3).broadcast_to([P, QT, NG, E1 // NG]), ALU.mult))
                    c(ts(ein[:, :, 0:E1], cw[:], 0.0, None, ALU.add))
                    c.hold()
                    for q in range(QT):
                        c.add(v.max(top[:, q, :], ein[:, q, 0:E1]))
                    c.wait()
                    c(v.memset(top[:, :, 4:8], PAD))
                    c.hold()
                    for q in range(QT):
                        c.add(v.match_replace(eout[:, q, :], top[:, q, :], ein[:, q, :], HIT))
                    c.wait()
                    c(stt(cw[:], eout[:, :, 0:E1], HIT, sco[:], ALU.is_equal, ALU.mult))
                    c(v.tensor_reduce(col[:], cw[:], AX, ALU.add))
                    c(ts(col[:], col[:], 1e-20, None, ALU.add))
                    c(v.reciprocal(col2[:], col[:]))
                    c(ts(col2[:], col2[:], 2.5, None, ALU.mult))
                    c(tt(cw[:], cw[:], col2[:].unsqueeze(2).broadcast_to([P, QT, E1]), ALU.mult))
                    c(v.tensor_copy(c3[:, :, 0, :], cw[:]))
                    c(tt(lsh[:], cw[:], c3[:, :, 0, :], ALU.subtract))
                    c(v.tensor_copy(c3[:, :, 1, :], lsh[:]))
                    tt(c3[:, :, 2, :], lsh[:], c3[:, :, 1, :], ALU.subtract).then_inc(s["d_c3"], 1)
                    assert c.n == c.per

            phases(dve, first, step_a, step_b, step_c, step_d)


def _consts():
    import numpy as np
    cf = np.zeros((P, P + 34), np.float32)
    cf[:, 0:P] = np.eye(P)
    for j in range(CH):
        for p in range(P):
            r = P * j + p
            if r < ROWS:
                cf[p, P + j * GH + r // NK] = 1
                cf[p, P + 20 + 2 * j + r // NK - FIRST[j]] = 1
    cf[:, P + 30:] = -0.5
    cb = np.zeros((P, 19 * P), np.float32)
    cb[:, 0:P] = np.eye(P)
    cb[:, P:2 * P] = np.triu(np.ones((P, P)), 1)
    cb[:, 2 * P:3 * P] = 1
    for e in range(E0):
        cb[e, (3 + e) * P:(4 + e) * P] = 1
    for t in range(RT):
        for part in range(3):
            for c in range(P):
                cb[part * E1 + 2 * t + c // 64, (11 + t) * P + c] = 1
    ko = np.zeros((2, 2, PW), np.float32)
    for a in range(2):
        for odd in range(2):
            ko[a, odd, odd * ODD + a * NK:odd * ODD + (a + 1) * NK] = 1
    one = 0x3F80
    return cf, (cb * one).astype(np.uint16), (ko * one).reshape(2, 2 * PW).astype(np.uint16)


_INS = ["x", "ctx_768", "L0_xattn_Wk", "L0_xattn_bk", "L0_xattn_Wv", "L0_xattn_bv", "L0_xattn_Wq", "L0_xattn_bq",
        "L0_xattn_Wo", "L0_xattn_bo", "L0_ffn_wg", "L0_ffn_W", "L0_ffn_b", "L1_xattn_Wq", "L1_xattn_Wk",
        "L1_xattn_Wv", "L1_xattn_Wo", "L1_xattn_bo", "L1_ffn_gate_w", "L1_ffn_bias_e", "L1_ffn_up_w",
        "L1_ffn_down_w", "L1_ffn_shared_up", "L1_ffn_shared_down"]


def kernel(**inputs):
    import numpy as _np
    import concourse.bacc as _bacc
    from concourse import mybir as _mybir
    from concourse.bass_utils import run_bass_kernel_spmd as _run

    nc = _bacc.Bacc("TRN2", target_bir_lowering=False, num_devices=1)
    arrays, args = {}, []
    for name in _INS:
        a = _np.ascontiguousarray(inputs[name])
        arrays[f"in_{name}"] = a
        args.append(nc.dram_tensor(f"in_{name}", a.shape, _mybir.dt.from_np(a.dtype), kind="ExternalInput").ap())
    for name, a in zip(("const_f", "const_b", "const_k"), _consts()):
        arrays[name] = a
        args.append(nc.dram_tensor(name, a.shape, _mybir.dt.from_np(a.dtype), kind="ExternalInput").ap())
    args.append(nc.dram_tensor("out", (B * NQ, D), F32, kind="ExternalOutput").ap())
    build(nc, *args)
    r = _run(nc, [arrays], core_ids=[0])
    return r.results[0]["out"].reshape(B, NQ, D)
```
